# Optimizing a Trainium2 kernel written in Bass

```python
import numpy as np
import jax
import jax.numpy as jnp

def _softmax(x, axis=-1):
    return jax.nn.softmax(x, axis=axis)

def _gelu(x):
    return jax.nn.gelu(x, approximate=True)

def _silu(x):
    return jax.nn.silu(x)

def _sigmoid(x):
    return jax.nn.sigmoid(x)

def _layernorm(x, axis=-1, eps=1e-05):
    m = jnp.mean(x, axis=axis, keepdims=True)
    v = jnp.var(x, axis=axis, keepdims=True)
    return (x - m) / jnp.sqrt(v + eps)

def _scatter_add(tgt, idx, src, axis=0):
    return tgt.at[idx].add(src)

def _segment_sum(src, seg, n):
    return jax.ops.segment_sum(src, seg, n)
kernel_name = 'mk_dlrm_tower_d1_rec_r8_e22437'

def setup_inputs(seed: int=0):
    np.random.seed(seed)
    _w = jnp.asarray

    def _rec_inputs():
        import jax
        import jax.numpy as jnp
        _tk = jax.random.key(seed)
        ids = jnp.stack([jax.random.randint(jax.random.fold_in(_tk, 200 + f), (2048,), 0, v, jnp.int32) for f, v in enumerate([12500, 12500, 1250, 125000, 12500, 12500, 1250, 12500, 1000, 1000, 1000, 1000, 12500, 1250, 12500, 1000, 1000, 1000, 1000, 1000, 12500, 12500, 1250, 1000, 1000, 1000])], axis=1)
        tbl_0 = 0.05 * jax.random.normal(jax.random.fold_in(_tk, 500 + 0), (12500, 128), jnp.float32)
        tbl_1 = 0.05 * jax.random.normal(jax.random.fold_in(_tk, 500 + 1), (12500, 128), jnp.float32)
        tbl_2 = 0.05 * jax.random.normal(jax.random.fold_in(_tk, 500 + 2), (1250, 128), jnp.float32)
        tbl_3 = 0.05 * jax.random.normal(jax.random.fold_in(_tk, 500 + 3), (125000, 128), jnp.float32)
        tbl_4 = 0.05 * jax.random.normal(jax.random.fold_in(_tk, 500 + 4), (12500, 128), jnp.float32)
        tbl_5 = 0.05 * jax.random.normal(jax.random.fold_in(_tk, 500 + 5), (12500, 128), jnp.float32)
        tbl_6 = 0.05 * jax.random.normal(jax.random.fold_in(_tk, 500 + 6), (1250, 128), jnp.float32)
        tbl_7 = 0.05 * jax.random.normal(jax.random.fold_in(_tk, 500 + 7), (12500, 128), jnp.float32)
        tbl_8 = 0.05 * jax.random.normal(jax.random.fold_in(_tk, 500 + 8), (1000, 128), jnp.float32)
        tbl_9 = 0.05 * jax.random.normal(jax.random.fold_in(_tk, 500 + 9), (1000, 128), jnp.float32)
        tbl_10 = 0.05 * jax.random.normal(jax.random.fold_in(_tk, 500 + 10), (1000, 128), jnp.float32)
        tbl_11 = 0.05 * jax.random.normal(jax.random.fold_in(_tk, 500 + 11), (1000, 128), jnp.float32)
        tbl_12 = 0.05 * jax.random.normal(jax.random.fold_in(_tk, 500 + 12), (12500, 128), jnp.float32)
        tbl_13 = 0.05 * jax.random.normal(jax.random.fold_in(_tk, 500 + 13), (1250, 128), jnp.float32)
        tbl_14 = 0.05 * jax.random.normal(jax.random.fold_in(_tk, 500 + 14), (12500, 128), jnp.float32)
        tbl_15 = 0.05 * jax.random.normal(jax.random.fold_in(_tk, 500 + 15), (1000, 128), jnp.float32)
        tbl_16 = 0.05 * jax.random.normal(jax.random.fold_in(_tk, 500 + 16), (1000, 128), jnp.float32)
        tbl_17 = 0.05 * jax.random.normal(jax.random.fold_in(_tk, 500 + 17), (1000, 128), jnp.float32)
        tbl_18 = 0.05 * jax.random.normal(jax.random.fold_in(_tk, 500 + 18), (1000, 128), jnp.float32)
        tbl_19 = 0.05 * jax.random.normal(jax.random.fold_in(_tk, 500 + 19), (1000, 128), jnp.float32)
        tbl_20 = 0.05 * jax.random.normal(jax.random.fold_in(_tk, 500 + 20), (12500, 128), jnp.float32)
        tbl_21 = 0.05 * jax.random.normal(jax.random.fold_in(_tk, 500 + 21), (12500, 128), jnp.float32)
        tbl_22 = 0.05 * jax.random.normal(jax.random.fold_in(_tk, 500 + 22), (1250, 128), jnp.float32)
        tbl_23 = 0.05 * jax.random.normal(jax.random.fold_in(_tk, 500 + 23), (1000, 128), jnp.float32)
        tbl_24 = 0.05 * jax.random.normal(jax.random.fold_in(_tk, 500 + 24), (1000, 128), jnp.float32)
        tbl_25 = 0.05 * jax.random.normal(jax.random.fold_in(_tk, 500 + 25), (1000, 128), jnp.float32)
        _rk = jax.random.fold_in(_tk, 7)
        r_dense_features = -0.000520686 + 1.00062 * jax.random.normal(jax.random.fold_in(_rk, 101), (2048, 128), jnp.float32)
        W_top1 = 0.0405887 * jax.random.normal(jax.random.fold_in(_tk, 801), (607, 512), jnp.float32)
        W_top2 = 0.0441942 * jax.random.normal(jax.random.fold_in(_tk, 802), (512, 256), jnp.float32)
        W_top3 = 0.0625 * jax.random.normal(jax.random.fold_in(_tk, 803), (256, 1), jnp.float32)
        b_top1 = jnp.zeros((512,), jnp.float32)
        b_top2 = jnp.zeros((256,), jnp.float32)
        return (r_dense_features, ids, tbl_0, tbl_1, tbl_2, tbl_3, tbl_4, tbl_5, tbl_6, tbl_7, tbl_8, tbl_9, tbl_10, tbl_11, tbl_12, tbl_13, tbl_14, tbl_15, tbl_16, tbl_17, tbl_18, tbl_19, tbl_20, tbl_21, tbl_22, tbl_23, tbl_24, tbl_25, W_top1, b_top1, W_top2, b_top2, W_top3)
    r_dense_features, ids, tbl_0, tbl_1, tbl_2, tbl_3, tbl_4, tbl_5, tbl_6, tbl_7, tbl_8, tbl_9, tbl_10, tbl_11, tbl_12, tbl_13, tbl_14, tbl_15, tbl_16, tbl_17, tbl_18, tbl_19, tbl_20, tbl_21, tbl_22, tbl_23, tbl_24, tbl_25, W_top1, b_top1, W_top2, b_top2, W_top3 = _rec_inputs()

    def _L0_rec_setup():
        import jax, jax.numpy as jnp
        import numpy as np
        F = 26
        N = F + 1
        _TRIU_I, _TRIU_J = np.triu_indices(N, k=1)
        key = jax.random.key(seed)
        k1, k2 = jax.random.split(key)
        B, D = (2048, 128)
        dense_features = jax.random.normal(k1, (B, D), dtype=jnp.float32)
        sparse_features = jax.random.normal(k2, (B, F, D), dtype=jnp.float32)
        return {'dense_features': dense_features, 'sparse_features': sparse_features}
    _L0_rec_all = _L0_rec_setup()
    _L0_rec_in = {k: v for k, v in _L0_rec_all.items() if k in ()}
    del _L0_rec_all
    return {'r_dense_features': r_dense_features, 'ids': ids, 'tbl_0': tbl_0, 'tbl_1': tbl_1, 'tbl_2': tbl_2, 'tbl_3': tbl_3, 'tbl_4': tbl_4, 'tbl_5': tbl_5, 'tbl_6': tbl_6, 'tbl_7': tbl_7, 'tbl_8': tbl_8, 'tbl_9': tbl_9, 'tbl_10': tbl_10, 'tbl_11': tbl_11, 'tbl_12': tbl_12, 'tbl_13': tbl_13, 'tbl_14': tbl_14, 'tbl_15': tbl_15, 'tbl_16': tbl_16, 'tbl_17': tbl_17, 'tbl_18': tbl_18, 'tbl_19': tbl_19, 'tbl_20': tbl_20, 'tbl_21': tbl_21, 'tbl_22': tbl_22, 'tbl_23': tbl_23, 'tbl_24': tbl_24, 'tbl_25': tbl_25, 'W_top1': W_top1, 'b_top1': b_top1, 'W_top2': W_top2, 'b_top2': b_top2, 'W_top3': W_top3}

def reference(r_dense_features, ids, tbl_0, tbl_1, tbl_2, tbl_3, tbl_4, tbl_5, tbl_6, tbl_7, tbl_8, tbl_9, tbl_10, tbl_11, tbl_12, tbl_13, tbl_14, tbl_15, tbl_16, tbl_17, tbl_18, tbl_19, tbl_20, tbl_21, tbl_22, tbl_23, tbl_24, tbl_25, W_top1, b_top1, W_top2, b_top2, W_top3):
    import jax
    import jax.numpy as jnp

    def _L0_rec_ref(dense_features, sparse_features):
        import jax, jax.numpy as jnp
        import numpy as np
        F = 26
        N = F + 1
        _TRIU_I, _TRIU_J = np.triu_indices(N, k=1)
        combined = jnp.concatenate([dense_features[:, None, :], sparse_features], axis=1)
        interactions = jnp.einsum('bnd,bmd->bnm', combined, combined)
        interactions_flat = interactions[:, _TRIU_I, _TRIU_J]
        return jnp.concatenate([dense_features, interactions_flat], axis=1)
    e = jnp.stack([tbl_0[ids[:, 0]], tbl_1[ids[:, 1]], tbl_2[ids[:, 2]], tbl_3[ids[:, 3]], tbl_4[ids[:, 4]], tbl_5[ids[:, 5]], tbl_6[ids[:, 6]], tbl_7[ids[:, 7]], tbl_8[ids[:, 8]], tbl_9[ids[:, 9]], tbl_10[ids[:, 10]], tbl_11[ids[:, 11]], tbl_12[ids[:, 12]], tbl_13[ids[:, 13]], tbl_14[ids[:, 14]], tbl_15[ids[:, 15]], tbl_16[ids[:, 16]], tbl_17[ids[:, 17]], tbl_18[ids[:, 18]], tbl_19[ids[:, 19]], tbl_20[ids[:, 20]], tbl_21[ids[:, 21]], tbl_22[ids[:, 22]], tbl_23[ids[:, 23]], tbl_24[ids[:, 24]], tbl_25[ids[:, 25]]], axis=1)
    z = _L0_rec_ref(r_dense_features, e)
    z = z.reshape(z.shape[0], -1)
    h = jnp.concatenate([z, r_dense_features], axis=1)
    h = jnp.maximum(h @ W_top1 + b_top1, 0.0)
    h = jnp.maximum(h @ W_top2 + b_top2, 0.0)
    y = h @ W_top3
    return y

_drawn_inputs = setup_inputs


def setup_inputs(seed=0):
    import zlib

    import numpy as np

    out = dict(_drawn_inputs(seed))
    spreads = {'b_top1': (0.0, 0.1), 'b_top2': (0.0, 0.1)}
    factors = {}
    for name, (base, spread) in spreads.items():
        noise = np.random.default_rng([zlib.crc32(name.encode()), seed]).standard_normal(out[name].shape)
        drawn = base * np.exp(spread * noise) if base else spread * noise
        out[name] = jnp.asarray(drawn.astype(out[name].dtype))
    for name, factor in factors.items():
        out[name] = (out[name] * factor).astype(out[name].dtype)
    return out
```

```python
import numpy as np
import concourse.bass as bass
from concourse import mybir
from contextlib import ExitStack

P = 128
D = 128
TABLES = 26
FEATURES = TABLES + 1
SLOT = 32
CHUNKS = 7
GROUP_OF = 4
GROUPS = -(-FEATURES // GROUP_OF)
STEPS = 4
BLOCKS = P // 4 // STEPS
BANK = 512
PER_BANK = 4
H1 = 512
H2 = 256


def features_of(group):
    return range(group * GROUP_OF, min(FEATURES, (group + 1) * GROUP_OF))


def build(nc, dense, ids, tables, w1_dense, w1_pairs, b1, w2, b2, w3, y):
    fp32 = mybir.dt.float32
    ALU = mybir.AluOpType
    ACT = mybir.ActivationFunctionType
    tiles = dense.shape[0] // P
    assert tiles % 2 == 0 and tiles >= 4

    ctx = ExitStack()
    with ctx:
        def sbuf(name, shape, dt=fp32):
            return ctx.enter_context(nc.sbuf_tensor(name, shape, dt))

        def psum(name, shape):
            return ctx.enter_context(nc.psum_tensor(name, shape, fp32))

        def sem(name):
            return ctx.enter_context(nc.semaphore(name))

        rows = [sbuf(f"rows{u}", [P, FEATURES, D]) for u in range(2)]
        index = [sbuf(f"index{u}", [P, TABLES], mybir.dt.int32) for u in range(2)]
        turned = [sbuf(f"turned{u}", [D, P, SLOT]) for u in range(2)]
        pairs = [sbuf(f"pairs{u}", [P, CHUNKS, P]) for u in range(2)]
        hidden1 = sbuf("hidden1", [P, H1 // P, P])
        hidden2 = sbuf("hidden2", [P, H2 // P, P])
        y_row = sbuf("y_row", [1, tiles * P])
        identity = sbuf("identity", [P, P])
        w1_dense_two = sbuf("w1_dense_two", [D, 2, H1])
        w1_dense_sum = sbuf("w1_dense_sum", [D, H1])
        w1_pairs_sb = sbuf("w1_pairs_sb", [P, CHUNKS, H1])
        w2_sb = sbuf("w2_sb", [P, H1 // P, H2])
        w3_sb = sbuf("w3_sb", [P, H2 // P])
        b1_sb = sbuf("b1_sb", [P, H1 // P])
        b2_sb = sbuf("b2_sb", [P, H2 // P])

        turn_ps = [psum(f"turn_ps{k}", [P, BANK]) for k in range(2)]
        gram_ps = [psum(f"gram_ps{k}", [P, BLOCKS // PER_BANK, BANK]) for k in range(2)]
        layer1_ps = psum("layer1_ps", [P, H1 // P, P])
        layer23_ps = psum("layer23_ps", [P, BANK // P, P])
        layer2_ps = layer23_ps[:, 0:H2 // P, :]
        layer3_ps = layer23_ps[0:1, H2 // P, :]

        weights_in = sem("weights_in")
        index_in = [sem(f"index_in{u}") for u in range(2)]
        dense_in = [sem(f"dense_in{u}") for u in range(2)]
        gathered = [[sem(f"gathered{u}_{g}") for g in range(GROUPS)] for u in range(2)]
        tiles_opened = sem("tiles_opened")
        identity_zero = sem("identity_zero")
        identity_made = sem("identity_made")
        padding_zero = sem("padding_zero")
        weights_summed = sem("weights_summed")
        turn_done = [sem(f"turn_done{u}") for u in range(2)]
        turned_dve = sem("turned_dve")
        turned_act = sem("turned_act")
        gram_done = sem("gram_done")
        pairs_dve = [sem(f"pairs_dve{k}") for k in range(2)]
        pairs_act = [sem(f"pairs_act{k}") for k in range(2)]
        layer1_done = sem("layer1_done")
        hidden1_ready = sem("hidden1_ready")
        layer2_done = sem("layer2_done")
        hidden2_ready = sem("hidden2_ready")
        layer3_done = sem("layer3_done")
        y_ready = sem("y_ready")
        y_stored = sem("y_stored")

        def bank_of(u, group):
            return (GROUPS * u + group) % 2

        def dve_groups(m, u, group):
            return GROUPS * m + (GROUPS * u + group + 1) // 2

        def act_groups(m, u, group):
            return GROUPS * m + (GROUPS * u + group) // 2

        block = ctx.enter_context(nc.Block())

        @block.sync
        def _(sp):
            def load_tile(m, u):
                t = 2 * m + u
                sp.wait_ge(turn_done[u], GROUPS * m)
                sp.dma_start(index[u][:], ids[bass.ts(t, P), :]).then_inc(index_in[u], 16)
                sp.dma_start(rows[u][:, 0, :], dense[bass.ts(t, P), :]).then_inc(dense_in[u], 16)

            load_tile(0, 0)
            load_tile(0, 1)
            sp.dma_start(w1_dense_two[:], w1_dense).then_inc(weights_in, 16)
            sp.dma_start(w1_pairs_sb[:], w1_pairs).then_inc(weights_in, 16)
            sp.dma_start(b1_sb[:], b1).then_inc(weights_in, 16)
            sp.dma_start(w2_sb[:], w2).then_inc(weights_in, 16)
            sp.dma_start(b2_sb[:], b2).then_inc(weights_in, 16)
            sp.dma_start(w3_sb[:], w3).then_inc(weights_in, 16)
            with sp.Fori(1, tiles // 2) as m:
                load_tile(m, 0)
                load_tile(m, 1)
            sp.wait_ge(y_ready, tiles)
            sp.dma_start(y, y_row[:]).then_inc(y_stored, 16)
            sp.wait_ge(y_stored, 16)

        @block.gpsimd
        def _(pool):
            nc.gpsimd.memset(identity[:], 0.0).then_inc(identity_zero, 1)
            pool.wait_ge(identity_zero, 1)
            nc.gpsimd.affine_select(out=identity[:], in_=identity[:], compare_op=ALU.not_equal, fill=1.0,
                                    base=0, pattern=[[-1, P]], channel_multiplier=1).then_inc(identity_made, 1)
            with pool.Fori(0, tiles // 2) as m:
                for u in range(2):
                    pool.wait_ge(turn_done[u], GROUPS * m)
                    pool.wait_ge(index_in[u], 16 * (m + 1))
                    pool.sem_inc(tiles_opened, 1)
                    for group in range(GROUPS):
                        for feature in features_of(group):
                            if feature > 0:
                                k = feature - 1
                                pool.indirect_dma_start(
                                    out=rows[u][:, feature, :], out_offset=None, in_=tables[k],
                                    in_offset=bass.IndirectOffsetOnAxis(ap=index[u][:, k:k + 1], axis=0),
                                ).then_inc(gathered[u][group], 16)

        @block.tensor
        def _(pe):
            def turn(m, u, group):
                bank = bank_of(u, group)
                fs = features_of(group)
                if bank == 0:
                    pe.wait_ge(turned_dve, dve_groups(m, u, group))
                else:
                    pe.wait_ge(turned_act, act_groups(m, u, group))
                if group == 0:
                    pe.wait_ge(dense_in[u], 16 * (m + 1))
                pe.wait_ge(gathered[u][group], 16 * (len(fs) - (group == 0)) * (m + 1))
                for n, feature in enumerate(fs):
                    last = nc.tensor.transpose(turn_ps[bank][:, n * P:(n + 1) * P], rows[u][:, feature, :],
                                               identity[:])
                last.then_inc(turn_done[u], 1)

            def gram(m, u, step):
                buf = step % 2
                if step == 0:
                    pe.wait_ge(turned_dve, dve_groups(m, u, GROUPS))
                    pe.wait_ge(turned_act, act_groups(m, u, GROUPS))
                pe.wait_ge(pairs_dve[buf], 2 * (2 * m + u) + step // 2)
                pe.wait_ge(pairs_act[buf], 2 * (2 * m + u) + step // 2)
                columns = turned[u][:, :, :].rearrange("d (g s) f -> d g (s f)", s=4)
                samples = turned[u][:, :, :].rearrange("d (g s) f -> d g s f", s=4)
                for b in range(BLOCKS):
                    g = step * BLOCKS + b
                    col = b % PER_BANK * 4 * FEATURES
                    last = nc.tensor.matmul(gram_ps[buf][:, b // PER_BANK, col:col + 4 * FEATURES],
                                            columns[:, g, :], samples[:, g, :, 0:FEATURES],
                                            start=True, stop=True)
                last.then_inc(gram_done, 1)

            def layer1(m, u):
                pe.wait_ge(pairs_dve[1], 2 * (2 * m + u) + 2)
                pe.wait_ge(pairs_act[1], 2 * (2 * m + u) + 2)
                for o in range(H1 // P):
                    nc.tensor.matmul(layer1_ps[:, o, :], w1_dense_sum[:, o * P:(o + 1) * P],
                                     turned[u][:, :, 0].rearrange("d (g s) -> d s g", s=4),
                                     start=True, stop=False)
                    for c in range(CHUNKS):
                        last = nc.tensor.matmul(layer1_ps[:, o, :], w1_pairs_sb[:, c, o * P:(o + 1) * P],
                                                pairs[u][:, c, :], start=False, stop=(c == CHUNKS - 1))
                last.then_inc(layer1_done, 1)

            def layer2(m, u):
                t = 2 * m + u
                pe.wait_ge(hidden1_ready, t + 1)
                pe.wait_ge(y_ready, t)
                for o in range(H2 // P):
                    for c in range(H1 // P):
                        last = nc.tensor.matmul(layer2_ps[:, o, :], w2_sb[:, c, o * P:(o + 1) * P],
                                                hidden1[:, c, :], start=(c == 0), stop=(c == H1 // P - 1))
                last.then_inc(layer2_done, 1)

            def layer3(m, u):
                pe.wait_ge(hidden2_ready, 2 * m + u + 1)
                for c in range(H2 // P):
                    last = nc.tensor.matmul(layer3_ps, w3_sb[:, c:c + 1], hidden2[:, c, :],
                                            start=(c == 0), stop=(c == H2 // P - 1))
                last.then_inc(layer3_done, 1)

            def tile(m, u, pm, pu):
                for group in range(GROUPS):
                    turn(m, u, group)
                    if group < STEPS:
                        gram(pm, pu, group)
                    elif group == 4:
                        layer1(pm, pu)
                    elif group == 5:
                        layer2(pm, pu)
                    else:
                        layer3(pm, pu)

            pe.wait_ge(identity_made, 1)
            for group in range(GROUPS):
                turn(0, 0, group)
            pe.wait_ge(padding_zero, 1)
            pe.wait_ge(weights_summed, 1)
            with pe.Fori(0, tiles // 2 - 1) as m:
                tile(m, 1, m, 0)
                tile(m + 1, 0, m, 1)
            last_m = tiles // 2 - 1
            tile(last_m, 1, last_m, 0)
            for step in range(STEPS):
                gram(last_m, 1, step)
            layer1(last_m, 1)
            layer2(last_m, 1)
            layer3(last_m, 1)

        def take_turned(eng, copy, done, m, u, group):
            eng.wait_ge(turn_done[u], GROUPS * m + group + 1)
            fs = features_of(group)
            n = len(fs)
            copy(turned[u][:, :, fs[0]:fs[0] + n],
                 turn_ps[bank_of(u, group)][:, 0:n * P].rearrange("d (f s) -> d s f", f=n)).then_inc(done, 1)

        def take_pairs(eng, copy, done, quadrants, m, u, step):
            buf = step % 2
            eng.wait_ge(gram_done, STEPS * (2 * m + u) + step + 1)
            for s in quadrants:
                blocks = gram_ps[buf][s * SLOT:(s + 1) * SLOT, :, 0:PER_BANK * 4 * FEATURES].rearrange(
                    "i k (b s j) -> i k b s j", b=PER_BANK, s=4)
                for q in range(4):
                    n = min(CHUNKS, FEATURES - q * CHUNKS)
                    sample = s * SLOT + step * BLOCKS
                    last = copy(
                        pairs[u][q * SLOT:(q + 1) * SLOT, 0:n, sample:sample + BLOCKS].rearrange(
                            "i c (k b) -> i k b c", k=BLOCKS // PER_BANK),
                        blocks[:, :, :, s, q * CHUNKS:q * CHUNKS + n])
            last.then_inc(done[buf], 1)

        @block.vector
        def _(dve):
            def turned_copy(m, u, group):
                if bank_of(u, group) == 0:
                    take_turned(dve, nc.vector.tensor_copy, turned_dve, m, u, group)

            def pairs_copy(m, u, step):
                take_pairs(dve, nc.vector.tensor_copy, pairs_dve, (0, 1), m, u, step)

            def relu2(m, u):
                dve.wait_ge(layer2_done, 2 * m + u + 1)
                for o in range(H2 // P):
                    last = nc.vector.tensor_scalar(hidden2[:, o, :], layer2_ps[:, o, :], b2_sb[:, o:o + 1], 0.0,
                                                   ALU.add, ALU.max)
                last.then_inc(hidden2_ready, 1)

            def y_copy(m, u):
                t = 2 * m + u
                dve.wait_ge(layer3_done, t + 1)
                nc.vector.tensor_copy(y_row[:, bass.ts(t, P)].rearrange("o (g s) -> o s g", s=4),
                                      layer3_ps.rearrange("o (s g) -> o s g", s=4)).then_inc(y_ready, 1)

            def tile(m, u, pm, pu):
                for group in range(GROUPS):
                    turned_copy(m, u, group)
                    if group < STEPS:
                        pairs_copy(pm, pu, group)
                    elif group == 5:
                        relu2(pm, pu)
                    elif group == 6:
                        y_copy(pm, pu)

            for u in range(2):
                last = nc.vector.memset(turned[u][:, :, FEATURES:SLOT], 0.0)
            for u in range(2):
                last = nc.vector.memset(pairs[u][3 * SLOT:4 * SLOT, CHUNKS - 1, :], 0.0)
            last.then_inc(padding_zero, 1)
            for group in range(GROUPS):
                turned_copy(0, 0, group)
                if group == 0:
                    dve.wait_ge(weights_in, 6 * 16)
                    nc.vector.tensor_tensor(w1_dense_sum[:], w1_dense_two[:, 0, :], w1_dense_two[:, 1, :],
                                            ALU.add).then_inc(weights_summed, 1)
            with dve.Fori(0, tiles // 2 - 1) as m:
                tile(m, 1, m, 0)
                tile(m + 1, 0, m, 1)
            last_m = tiles // 2 - 1
            tile(last_m, 1, last_m, 0)
            for step in range(STEPS):
                pairs_copy(last_m, 1, step)
            relu2(last_m, 1)
            y_copy(last_m, 1)

        @block.scalar
        def _(act):
            def turned_copy(m, u, group):
                if bank_of(u, group) == 1:
                    take_turned(act, nc.scalar.copy, turned_act, m, u, group)

            def pairs_copy(m, u, step):
                take_pairs(act, nc.scalar.copy, pairs_act, (2, 3), m, u, step)

            def relu1(m, u):
                act.wait_ge(layer1_done, 2 * m + u + 1)
                for o in range(H1 // P):
                    last = nc.scalar.activation(hidden1[:, o, :], layer1_ps[:, o, :], ACT.Relu,
                                                bias=b1_sb[:, o:o + 1])
                last.then_inc(hidden1_ready, 1)

            def tile(m, u, pm, pu):
                for group in range(GROUPS):
                    turned_copy(m, u, group)
                    if group < STEPS:
                        pairs_copy(pm, pu, group)
                    elif group == 4:
                        relu1(pm, pu)

            for group in range(GROUPS):
                turned_copy(0, 0, group)
            act.wait_ge(weights_in, 6 * 16)
            with act.Fori(0, tiles // 2 - 1) as m:
                tile(m, 1, m, 0)
                tile(m + 1, 0, m, 1)
            last_m = tiles // 2 - 1
            tile(last_m, 1, last_m, 0)
            for step in range(STEPS):
                pairs_copy(last_m, 1, step)
            relu1(last_m, 1)


def kernel(**inputs):
    import concourse.bacc as bacc
    from concourse.bass_utils import run_bass_kernel_spmd

    a = {name: np.ascontiguousarray(value) for name, value in inputs.items()}
    w1, w2, w3 = a["W_top1"], a["W_top2"], a["W_top3"]
    n_pairs = FEATURES * (FEATURES - 1) // 2

    w1_dense = np.stack([w1[:D], w1[D + n_pairs:]], axis=1)
    w1_pairs = np.zeros((P, CHUNKS, H1), w1.dtype)
    row = D
    for i in range(FEATURES):
        for j in range(i + 1, FEATURES):
            w1_pairs[j // CHUNKS * SLOT + i, j % CHUNKS] = w1[row]
            row += 1

    arrays = {
        "dense": a["r_dense_features"], "ids": a["ids"],
        **{f"table{k}": a[f"tbl_{k}"] for k in range(TABLES)},
        "w1_dense": w1_dense, "w1_pairs": w1_pairs,
        "b1": np.ascontiguousarray(a["b_top1"].reshape(-1, P).T),
        "w2": np.ascontiguousarray(w2.reshape(-1, P, H2).transpose(1, 0, 2)),
        "b2": np.ascontiguousarray(a["b_top2"].reshape(-1, P).T),
        "w3": np.ascontiguousarray(w3.reshape(-1, P).T),
    }
    nc = bacc.Bacc("TRN2", target_bir_lowering=False, num_devices=1)
    ap = {name: nc.dram_tensor(f"in_{name}", v.shape, mybir.dt.from_np(v.dtype), kind="ExternalInput").ap()
          for name, v in arrays.items()}
    batch = a["ids"].shape[0]
    y = nc.dram_tensor("out_y", (1, batch), mybir.dt.float32, kind="ExternalOutput").ap()
    build(nc, ap["dense"], ap["ids"], [ap[f"table{k}"] for k in range(TABLES)], ap["w1_dense"], ap["w1_pairs"],
          ap["b1"], ap["w2"], ap["b2"], ap["w3"], y)
    result = run_bass_kernel_spmd(nc, [{f"in_{name}": v for name, v in arrays.items()}], core_ids=[0])
    return result.results[0]["out_y"].reshape(batch, 1)
```

```python
import numpy as np
import concourse.bass as bass
from concourse import mybir
from contextlib import ExitStack

P = 128
D = 128
TABLES = 26
FEATURES = TABLES + 1
SLOT = 28
LOOKED = [8, 9, 10, 11, 15, 16]
GATHERED = [k for k in range(TABLES) if k not in LOOKED]
LOOKS = len(LOOKED)
PARTS = 8
GROUP_OF = 4
GROUPS = -(-len(GATHERED) // GROUP_OF)
STEPS = 2
IN_QUADRANT = P // STEPS // 4
SHIFTS = (FEATURES - 1) // 2
CHUNK_I = 9
CHUNKS = FEATURES // CHUNK_I
CHUNK_ROWS = CHUNK_I * SHIFTS
BANK = 512
H1 = 512
H2 = 256
L1 = H1 // P
L2 = H2 // P


def tables_of(group):
    return GATHERED[group * GROUP_OF:(group + 1) * GROUP_OF]


def runs_of(group):
    runs = []
    for n, k in enumerate(tables_of(group)):
        if runs and runs[-1][1] + runs[-1][2] == k:
            runs[-1][2] += 1
        else:
            runs.append([n, k, 1])
    return runs


def looks_after(group):
    return [r for r in range(LOOKS) if 1 + r * (GROUPS - 1) // LOOKS == group]


def build(nc, dense_t, ids, ids_t, tables, w1_dense, w1_pairs, b1, w2, b2, w3, y):
    fp32, fp32r, int32 = mybir.dt.float32, mybir.dt.float32r, mybir.dt.int32
    ALU = mybir.AluOpType
    ACT = mybir.ActivationFunctionType
    batch = ids.shape[0]
    tiles = batch // P
    assert batch % (2 * P) == 0 and tiles >= 6
    look_rows = tables[LOOKED[0]].shape[0] // PARTS
    assert all(tables[k].shape[0] == look_rows * PARTS for k in LOOKED)
    assert look_rows <= P and look_rows * PARTS <= 4096

    ctx = ExitStack()
    with ctx:
        def sbuf(name, shape, dt=fp32):
            return ctx.enter_context(nc.sbuf_tensor(name, shape, dt))

        def psum(name, shape):
            return ctx.enter_context(nc.psum_tensor(name, shape, fp32))

        def sem(name):
            return ctx.enter_context(nc.semaphore(name))

        rows = [sbuf(f"rows{u}", [P, len(GATHERED), D]) for u in range(2)]
        index = [sbuf(f"index{u}", [P, TABLES], int32) for u in range(2)]
        turned = sbuf("turned", [D, 2, P, SLOT])
        grams = [sbuf(f"grams{u}", [P, FEATURES, P]) for u in range(2)]
        pairs = [sbuf(f"pairs{u}", [P, CHUNKS, P]) for u in range(2)]
        hidden1 = sbuf("hidden1", [P, L1, P])
        hidden2 = sbuf("hidden2", [P, L2, P])
        y_row = sbuf("y_row", [1, batch])
        dense_sb = sbuf("dense_sb", [D, batch])
        identity = sbuf("identity", [P, P])
        look_ids_int = sbuf("look_ids_int", [LOOKS, batch], int32)
        look_ids = sbuf("look_ids", [P, batch], fp32r)
        spreader_made = sbuf("spreader_made", [P, LOOKS, P])
        spreader = sbuf("spreader", [P, LOOKS, P], fp32r)
        row_number_int = sbuf("row_number_int", [P, PARTS], int32)
        row_number = sbuf("row_number", [P, PARTS])
        table_high = sbuf("table_high", [P, LOOKS, PARTS, D], fp32r)
        table_low = sbuf("table_low", [P, LOOKS, PARTS, D], fp32r)
        match = [sbuf(f"match{b}", [P, PARTS, 2 * P], fp32r) for b in range(2)]
        w1_dense_two = sbuf("w1_dense_two", [D, 2, H1])
        w1_dense_sum = sbuf("w1_dense_sum", [D, H1])
        w1_pairs_sb = sbuf("w1_pairs_sb", [CHUNK_ROWS, CHUNKS, H1])
        w2_sb = sbuf("w2_sb", [P, L1, H2])
        w3_sb = sbuf("w3_sb", [P, L2])
        b1_sb = sbuf("b1_sb", [P, L1])
        b2_sb = sbuf("b2_sb", [P, L2])
        scratch = [nc.dram_tensor(f"scratch{u}", (FEATURES, FEATURES + SHIFTS, P), fp32).ap() for u in range(2)]

        def raw_table(n):
            flat = grams[n % 2][0:look_rows].rearrange("p j s -> p (j s)")
            at = n // 2 * PARTS * D
            assert at + PARTS * D <= FEATURES * P
            return flat[:, at:at + PARTS * D]

        turn_ps = [psum(f"turn_ps{b}", [P, BANK]) for b in range(2)]
        gram_ps = [psum(f"gram_ps{b}", [P, BANK]) for b in range(2)]
        layer1_ps = psum("layer1_ps", [P, L1, P])
        layer23_ps = psum("layer23_ps", [P, BANK // P, P])
        layer2_ps = layer23_ps[:, 0:L2, :]
        layer3_ps = layer23_ps[0:1, L2, :]
        spread_ps = psum("spread_ps", [P, BANK])
        look_ps = psum("look_ps", [P, BANK])

        index_in = [sem(f"index_in{u}") for u in range(2)]
        look_ids_in = sem("look_ids_in")
        raw_tables_in = sem("raw_tables_in")
        dense_in = sem("dense_in")
        weights_in = sem("weights_in")
        gathered = [[sem(f"gathered{u}_{g}") for g in range(GROUPS)] for u in range(2)]
        tiles_opened = sem("tiles_opened")
        zeroed = sem("zeroed")
        identity_made = sem("identity_made")
        look_constants_made = sem("look_constants_made")
        look_constants_ready = sem("look_constants_ready")
        look_ids_zero = sem("look_ids_zero")
        look_ids_ready = sem("look_ids_ready")
        tables_high = sem("tables_high")
        tables_split = sem("tables_split")
        weights_summed = sem("weights_summed")
        turn_done = [sem(f"turn_done{u}") for u in range(2)]
        turned_dve = sem("turned_dve")
        turned_act = sem("turned_act")
        spread_done = sem("spread_done")
        match_ready = sem("match_ready")
        look_done = sem("look_done")
        looked = sem("looked")
        gram_done = sem("gram_done")
        grams_dve = sem("grams_dve")
        grams_act = sem("grams_act")
        scratch_in = [sem(f"scratch_in{u}") for u in range(2)]
        pairs_in = [sem(f"pairs_in{u}") for u in range(2)]
        layer1_done = sem("layer1_done")
        hidden1_ready = sem("hidden1_ready")
        layer2_done = sem("layer2_done")
        hidden2_ready = sem("hidden2_ready")
        layer3_done = sem("layer3_done")
        y_copied = sem("y_copied")
        y_stored = sem("y_stored")

        WRITES, READS = 2 * 16, CHUNKS * 16

        def after(eng, sem, count):
            if not isinstance(count, int) or count > 0:
                eng.wait_ge(sem, count)

        def bank_of(u, group):
            return (GROUPS * u + group) % 2

        def groups_in_bank(bank, m, u, group):
            return GROUPS * m + (GROUPS * u + group + 1 - bank) // 2

        block = ctx.enter_context(nc.Block())

        @block.sync
        def _(sp):
            def known(value):
                return value if isinstance(value, int) else sp.snap(sp.to_reg(value))

            def load_index(m, u):
                first = known((2 * m + u) * P)
                after(sp, turn_done[u], known(GROUPS * m))
                sp.dma_start(index[u][:], ids[bass.ds(first, P), :]).then_inc(index_in[u], 16)

            def repack(m, u):
                t = 2 * m + u
                copied, reads, writes, layer1s = (
                    known(v) for v in (STEPS * (t + 1), READS * m, WRITES * (m + 1), t - 1))
                sp.wait_ge(grams_dve, copied)
                sp.wait_ge(grams_act, copied)
                after(sp, pairs_in[u], reads)
                sp.dma_start(scratch[u][:, 0:FEATURES, :], grams[u][0:FEATURES]).then_inc(scratch_in[u], 16)
                sp.dma_start(scratch[u][:, FEATURES:, :],
                             grams[u][0:FEATURES, 0:SHIFTS, :]).then_inc(scratch_in[u], 16)
                sp.wait_ge(scratch_in[u], writes)
                after(sp, layer1_done, layer1s)
                width = FEATURES + SHIFTS
                for c in range(CHUNKS):
                    first = c * CHUNK_I * (width + 1) + 1
                    skewed = bass.AP(scratch[u].tensor, first * P, [[(width + 1) * P, CHUNK_I], [P, SHIFTS], [1, P]])
                    sp.dma_start(pairs[u][0:CHUNK_ROWS, c, :], skewed).then_inc(pairs_in[u], 16)

            load_index(0, 0)
            load_index(0, 1)
            for n, k in enumerate(LOOKED):
                sp.dma_start(look_ids_int[n:n + 1, :], ids_t[k:k + 1, :]).then_inc(look_ids_in, 16)
            for n, k in enumerate(LOOKED):
                sp.dma_start(raw_table(n), tables[k].rearrange("(p c) d -> p (c d)", c=PARTS)).then_inc(
                    raw_tables_in, 16)
            sp.dma_start(dense_sb[:], dense_t).then_inc(dense_in, 16)
            sp.dma_start(w1_dense_two[:], w1_dense).then_inc(weights_in, 16)
            sp.dma_start(w1_pairs_sb[:], w1_pairs).then_inc(weights_in, 16)
            sp.dma_start(b1_sb[:], b1).then_inc(weights_in, 16)
            sp.dma_start(w2_sb[:], w2).then_inc(weights_in, 16)
            sp.dma_start(b2_sb[:], b2).then_inc(weights_in, 16)
            sp.dma_start(w3_sb[:], w3).then_inc(weights_in, 16)
            for u in range(2):
                load_index(1, u)
                repack(0, u)
            with sp.Fori(2, tiles // 2) as m:
                for u in range(2):
                    load_index(m, u)
                    repack(m - 1, u)
            for u in range(2):
                repack(tiles // 2 - 1, u)
            sp.wait_ge(y_copied, tiles + 1)
            sp.dma_start(y, y_row[:]).then_inc(y_stored, 16)
            sp.wait_ge(y_stored, 16)

        @block.gpsimd
        def _(pool):
            def gather_tile(m, u):
                after(pool, turn_done[u], GROUPS * m)
                pool.wait_ge(index_in[u], 16 * (m + 1))
                pool.sem_inc(tiles_opened, 1)
                for group in range(GROUPS):
                    for n, k in enumerate(tables_of(group)):
                        pool.indirect_dma_start(
                            out=rows[u][:, group * GROUP_OF + n, :], out_offset=None, in_=tables[k],
                            in_offset=bass.IndirectOffsetOnAxis(ap=index[u][:, k:k + 1], axis=0),
                        ).then_inc(gathered[u][group], 16)

            nc.gpsimd.memset(identity[:], 0.0).then_inc(zeroed, 1)
            nc.gpsimd.memset(spreader_made[:], 0.0).then_inc(zeroed, 1)
            pool.wait_ge(zeroed, 2)
            nc.gpsimd.affine_select(out=identity[:], in_=identity[:], compare_op=ALU.not_equal, fill=1.0,
                                    base=0, pattern=[[-1, P]], channel_multiplier=1).then_inc(identity_made, 1)
            nc.gpsimd.affine_select(out=spreader_made[:], in_=spreader_made[:], compare_op=ALU.not_equal,
                                    fill=1.0, base=0, pattern=[[-1, LOOKS], [0, P]],
                                    channel_multiplier=1).then_inc(look_constants_made, 1)
            nc.gpsimd.iota(row_number_int[:], pattern=[[1, PARTS]], base=0,
                           channel_multiplier=PARTS).then_inc(look_constants_made, 1)
            gather_tile(0, 0)
            gather_tile(0, 1)
            with pool.Fori(1, tiles // 2) as m:
                gather_tile(m, 0)
                gather_tile(m, 1)

        @block.tensor
        def _(pe):
            def turn(m, u, group):
                bank = bank_of(u, group)
                after(pe, (turned_dve, turned_act)[bank], groups_in_bank(bank, m, u, group))
                ks = tables_of(group)
                pe.wait_ge(gathered[u][group], 16 * len(ks) * (m + 1))
                for n in range(len(ks)):
                    last = nc.tensor.transpose(turn_ps[bank][:, n * P:(n + 1) * P],
                                               rows[u][:, group * GROUP_OF + n, :], identity[:])
                last.then_inc(turn_done[u], 1)

            def spread(m, r):
                after(pe, match_ready, LOOKS * m + r)
                nc.tensor.matmul(spread_ps[:, 0:2 * P], spreader[:, r, :], look_ids[:, bass.ts(m, 2 * P)],
                                 start=True, stop=True).then_inc(spread_done, 1)

            def look(m, r):
                if r + 1 < LOOKS:
                    spread(m, r + 1)
                pe.wait_ge(match_ready, LOOKS * m + r + 1)
                after(pe, looked, LOOKS * m + r)
                for c in range(PARTS):
                    for part in (table_high, table_low):
                        last = nc.tensor.matmul(look_ps[:, 0:2 * P], part[0:look_rows, r, c, :],
                                                match[r % 2][0:look_rows, c, :],
                                                start=(c == 0 and part is table_high),
                                                stop=(c == PARTS - 1 and part is table_low))
                last.then_inc(look_done, 1)

            def gram(m, u, step):
                t = 2 * m + u
                if step == 0:
                    pe.wait_ge(turned_dve, groups_in_bank(0, m, u, GROUPS))
                    pe.wait_ge(turned_act, groups_in_bank(1, m, u, GROUPS))
                    pe.wait_ge(looked, LOOKS * (m + 1))
                after(pe, grams_dve, STEPS * t + step - 1)
                after(pe, grams_act, STEPS * t + step - 1)
                for s in range(4):
                    for x in range(IN_QUADRANT):
                        of_sample = turned[:, u, (step * 4 + s) * IN_QUADRANT + x, 0:FEATURES]
                        last = nc.tensor.matmul(
                            gram_ps[step][s * 32:s * 32 + FEATURES, x * FEATURES:(x + 1) * FEATURES],
                            of_sample, of_sample, start=True, stop=True)
                last.then_inc(gram_done, 1)

            def layer1(m, u):
                pe.wait_ge(pairs_in[u], READS * (m + 1))
                for o in range(L1):
                    nc.tensor.matmul(layer1_ps[:, o, :], w1_dense_sum[:, o * P:(o + 1) * P],
                                     dense_sb[:, bass.ts(2 * m + u, P)], start=True, stop=False)
                    for c in range(CHUNKS):
                        last = nc.tensor.matmul(layer1_ps[:, o, :], w1_pairs_sb[:, c, o * P:(o + 1) * P],
                                                pairs[u][0:CHUNK_ROWS, c, :],
                                                start=False, stop=(c == CHUNKS - 1))
                last.then_inc(layer1_done, 1)

            def layer2(m, u):
                t = 2 * m + u
                pe.wait_ge(hidden1_ready, t + 1)
                pe.wait_ge(y_copied, t + 1)
                for o in range(L2):
                    for c in range(L1):
                        last = nc.tensor.matmul(layer2_ps[:, o, :], w2_sb[:, c, o * P:(o + 1) * P],
                                                hidden1[:, c, :], start=(c == 0), stop=(c == L1 - 1))
                last.then_inc(layer2_done, 1)

            def layer3(m, u):
                pe.wait_ge(hidden2_ready, 2 * m + u + 1)
                for c in range(L2):
                    last = nc.tensor.matmul(layer3_ps, w3_sb[:, c:c + 1], hidden2[:, c, :],
                                            start=(c == 0), stop=(c == L2 - 1))
                last.then_inc(layer3_done, 1)

            def tile(m, u, grams=True, layers=True):
                gm = m - 1 + u
                if u == 0:
                    spread(m, 0)
                for group in range(GROUPS):
                    turn(m, u, group)
                    if grams and group < STEPS:
                        gram(gm, 1 - u, group)
                    if layers and group == GROUPS - 3:
                        layer1(m - 1, u)
                    if layers and group == GROUPS - 2:
                        layer2(m - 1, u)
                    if layers and group == GROUPS - 1:
                        layer3(m - 1, u)
                    if u == 0:
                        for r in looks_after(group):
                            look(m, r)

            pe.wait_ge(identity_made, 1)
            pe.wait_ge(look_ids_ready, 1)
            pe.wait_ge(look_constants_ready, 1)
            pe.wait_ge(tables_split, LOOKS)
            tile(0, 0, grams=False, layers=False)
            tile(0, 1, layers=False)
            pe.wait_ge(weights_summed, 1)
            pe.wait_ge(dense_in, 16)
            with pe.Fori(1, tiles // 2) as m:
                tile(m, 0)
                tile(m, 1)
            last_m = tiles // 2 - 1
            for step in range(STEPS):
                gram(last_m, 1, step)
            for u in range(2):
                layer1(last_m, u)
                layer2(last_m, u)
                layer3(last_m, u)

        def take_turned(eng, copy, done, m, u, group):
            eng.wait_ge(turn_done[u], GROUPS * m + group + 1)
            bank = turn_ps[bank_of(u, group)]
            for n, k, length in runs_of(group):
                last = copy(turned[:, u, :, 1 + k:1 + k + length],
                            bank[:, n * P:(n + length) * P].rearrange("d (f s) -> d s f", f=length))
            last.then_inc(done, 1)

        def take_gram(eng, copy, done, quadrants, m, u, step):
            eng.wait_ge(gram_done, STEPS * (2 * m + u) + step + 1)
            if step == 0:
                after(eng, scratch_in[u], WRITES * m)
            for s in quadrants:
                sample = (step * 4 + s) * IN_QUADRANT
                last = copy(grams[u][0:FEATURES, :, sample:sample + IN_QUADRANT],
                            gram_ps[step][s * 32:s * 32 + FEATURES, 0:IN_QUADRANT * FEATURES].rearrange(
                                "i (x j) -> i j x", j=FEATURES))
            last.then_inc(done, 1)

        @block.vector
        def _(dve):
            def matches(m, r):
                dve.wait_ge(spread_done, LOOKS * m + r + 1)
                before = LOOKS * m + r - 2 if r >= 2 else LOOKS * (m - 1) + max(
                    q for q in range(LOOKS) if q % 2 == r)
                after(dve, look_done, before + 1)
                shape = [look_rows, PARTS, 2 * P]
                nc.vector.tensor_tensor(
                    match[r % 2][0:look_rows], spread_ps[0:look_rows, 0:2 * P].unsqueeze(1).broadcast_to(shape),
                    row_number[0:look_rows].unsqueeze(2).broadcast_to(shape),
                    ALU.is_equal).then_inc(match_ready, 1)

            def relu2(m, u):
                dve.wait_ge(layer2_done, 2 * m + u + 1)
                for o in range(L2):
                    last = nc.vector.tensor_scalar(hidden2[:, o, :], layer2_ps[:, o, :], b2_sb[:, o:o + 1], 0.0,
                                                   ALU.add, ALU.max)
                last.then_inc(hidden2_ready, 1)

            def copy_y(m, u):
                t = 2 * m + u
                dve.wait_ge(layer3_done, t + 1)
                nc.vector.tensor_copy(y_row[:, bass.ts(t, P)], layer3_ps).then_inc(y_copied, 1)

            def take_steps(m, u, step):
                take_gram(dve, nc.vector.tensor_copy, grams_dve, (0, 1), m, u, step)

            def tile(m, u, grams=True, layers=True):
                gm = m - 1 + u
                if u == 0:
                    matches(m, 0)
                for group in range(GROUPS):
                    if bank_of(u, group) == 0:
                        take_turned(dve, nc.vector.tensor_copy, turned_dve, m, u, group)
                    if grams and group < STEPS:
                        take_steps(gm, 1 - u, group)
                    if layers and group == GROUPS - 2:
                        relu2(m - 1, u)
                    if layers and group == GROUPS - 1:
                        copy_y(m - 1, u)
                    if u == 0:
                        for r in looks_after(group):
                            if r + 1 < LOOKS:
                                matches(m, r + 1)

            dve.sem_inc(y_copied, 1)
            nc.vector.memset(look_ids[:].bitcast(fp32), 0.0).then_inc(look_ids_zero, 1)
            dve.wait_ge(look_constants_made, 2)
            nc.vector.tensor_copy(spreader[:], spreader_made[:])
            nc.vector.tensor_copy(row_number[:], row_number_int[:]).then_inc(look_constants_ready, 1)
            dve.wait_ge(look_ids_zero, 1)
            dve.wait_ge(look_ids_in, 16 * LOOKS)
            nc.vector.tensor_copy(look_ids[0:LOOKS], look_ids_int[:]).then_inc(look_ids_ready, 1)
            for n in range(LOOKS):
                dve.wait_ge(tables_high, n + 1)
                nc.vector.tensor_tensor(table_low[0:look_rows, n].rearrange("p c d -> p (c d)"), raw_table(n),
                                        table_high[0:look_rows, n].bitcast(fp32).rearrange("p c d -> p (c d)"),
                                        ALU.subtract).then_inc(tables_split, 1)
            dve.wait_ge(look_constants_ready, 1)
            tile(0, 0, grams=False, layers=False)
            dve.wait_ge(weights_in, 6 * 16)
            nc.vector.tensor_tensor(w1_dense_sum[:], w1_dense_two[:, 0, :], w1_dense_two[:, 1, :],
                                    ALU.add).then_inc(weights_summed, 1)
            tile(0, 1, layers=False)
            with dve.Fori(1, tiles // 2) as m:
                tile(m, 0)
                tile(m, 1)
            last_m = tiles // 2 - 1
            for step in range(STEPS):
                take_steps(last_m, 1, step)
            for u in range(2):
                relu2(last_m, u)
                copy_y(last_m, u)

        @block.scalar
        def _(act):
            def relu1(m, u):
                act.wait_ge(layer1_done, 2 * m + u + 1)
                for o in range(L1):
                    last = nc.scalar.activation(hidden1[:, o, :], layer1_ps[:, o, :], ACT.Relu,
                                                bias=b1_sb[:, o:o + 1])
                last.then_inc(hidden1_ready, 1)

            def take_look(m, r):
                act.wait_ge(look_done, LOOKS * m + r + 1)
                if r == 0:
                    nc.scalar.copy(turned[:, :, :, 0],
                                   dense_sb[:, bass.ts(m, 2 * P)].rearrange("d (u s) -> d u s", u=2))
                nc.scalar.copy(turned[:, :, :, 1 + LOOKED[r]],
                               look_ps[:, 0:2 * P].rearrange("d (u s) -> d u s", u=2)).then_inc(looked, 1)

            def take_steps(m, u, step):
                take_gram(act, nc.scalar.copy, grams_act, (2, 3), m, u, step)

            def tile(m, u, grams=True, layers=True):
                gm = m - 1 + u
                for group in range(GROUPS):
                    if bank_of(u, group) == 1:
                        take_turned(act, nc.scalar.copy, turned_act, m, u, group)
                    if grams and group < STEPS:
                        take_steps(gm, 1 - u, group)
                    if layers and group == GROUPS - 3:
                        relu1(m - 1, u)
                    if u == 0:
                        for r in looks_after(group):
                            take_look(m, r)

            for n in range(LOOKS):
                act.wait_ge(raw_tables_in, 16 * LOOKS)
                nc.scalar.copy(table_high[0:look_rows, n].rearrange("p c d -> p (c d)"),
                               raw_table(n)).then_inc(tables_high, 1)
            act.wait_ge(dense_in, 16)
            tile(0, 0, grams=False, layers=False)
            tile(0, 1, layers=False)
            act.wait_ge(weights_in, 6 * 16)
            with act.Fori(1, tiles // 2) as m:
                tile(m, 0)
                tile(m, 1)
            last_m = tiles // 2 - 1
            for step in range(STEPS):
                take_steps(last_m, 1, step)
            for u in range(2):
                relu1(last_m, u)


def kernel(**inputs):
    import concourse.bacc as bacc
    from concourse.bass_utils import run_bass_kernel_spmd

    a = {name: np.ascontiguousarray(value) for name, value in inputs.items()}
    w1, w2, w3 = a["W_top1"], a["W_top2"], a["W_top3"]
    batch = a["ids"].shape[0]

    n_pairs = FEATURES * (FEATURES - 1) // 2
    w1_dense = np.stack([w1[:D], w1[D + n_pairs:]], axis=1)
    row_of = {}
    for i in range(FEATURES):
        for j in range(i + 1, FEATURES):
            row_of[i, j] = D + len(row_of)
    order = [row_of[min(i, (i + s) % FEATURES), max(i, (i + s) % FEATURES)]
             for i in range(FEATURES) for s in range(1, SHIFTS + 1)]
    w1_pairs = w1[order].reshape(CHUNKS, CHUNK_ROWS, H1).transpose(1, 0, 2)

    arrays = {
        "dense_t": a["r_dense_features"].T, "ids": a["ids"], "ids_t": a["ids"].T,
        **{f"table{k}": a[f"tbl_{k}"] for k in range(TABLES)},
        "w1_dense": w1_dense, "w1_pairs": w1_pairs, "b1": a["b_top1"].reshape(L1, P).T,
        "w2": w2.reshape(L1, P, H2).transpose(1, 0, 2), "b2": a["b_top2"].reshape(L2, P).T,
        "w3": w3.reshape(L2, P).T,
    }
    arrays = {name: np.ascontiguousarray(v) for name, v in arrays.items()}
    nc = bacc.Bacc("TRN2", target_bir_lowering=False, num_devices=1)
    ap = {name: nc.dram_tensor(f"in_{name}", v.shape, mybir.dt.from_np(v.dtype), kind="ExternalInput").ap()
          for name, v in arrays.items()}
    y = nc.dram_tensor("out_y", (1, batch), mybir.dt.float32, kind="ExternalOutput").ap()
    build(nc, ap["dense_t"], ap["ids"], ap["ids_t"], [ap[f"table{k}"] for k in range(TABLES)],
          ap["w1_dense"], ap["w1_pairs"], ap["b1"], ap["w2"], ap["b2"], ap["w3"], y)
    result = run_bass_kernel_spmd(nc, [{f"in_{name}": v for name, v in arrays.items()}], core_ids=[0])
    return result.results[0]["out_y"].reshape(batch, 1)
```

```python
import numpy as np
import concourse.bass as bass
from concourse import mybir
from contextlib import ExitStack

P = 128
D = 128
TABLES = 26
FEATURES = TABLES + 1
SLOT = 28
LOOKED = [8, 9, 10, 11, 15, 16, 17, 18]
GATHERED = [k for k in range(TABLES) if k not in LOOKED]
LOOKS = len(LOOKED)
HALF = LOOKS // 2
EARLY = 2
STAGED = LOOKS - 2
PARTS = 8
GROUP_OF = 4
GROUPS = -(-len(GATHERED) // GROUP_OF)
STEPS = 2
AT_LAYER = [1, 2, 3]
IN_QUADRANT = P // STEPS // 4
SHIFTS = (FEATURES - 1) // 2
WRAPS = FEATURES - SHIFTS
CHUNK_I = 9
CHUNKS = FEATURES // CHUNK_I
CHUNK_ROWS = CHUNK_I * SHIFTS
BANK = 512
H1 = 512
H2 = 256
L1 = H1 // P
L2 = H2 // P


def tables_of(group):
    return GATHERED[group * GROUP_OF:(group + 1) * GROUP_OF]


def runs_of(some_tables):
    runs = []
    for n, k in enumerate(some_tables):
        if runs and runs[-1][1] + runs[-1][2] == k:
            runs[-1][2] += 1
        else:
            runs.append([n, k, 1])
    return runs


def looks_after(m, u, group):
    looks = [(m + 1, r) for r in range(HALF)] if u else [(m, r) for r in range(HALF, LOOKS)]
    if isinstance(m, int) and m + u == 0:
        looks = [(0, r) for r in range(EARLY, LOOKS)]
        return [look for n, look in enumerate(looks) if n * GROUPS // len(looks) == group]
    return [look for n, look in enumerate(looks) if n * (GROUPS - 1) // len(looks) == group]


def build(nc, dense_t, ids, look_ids_rows, tables, w1_dense, w1_pairs, b1, w2, b2, w3, y):
    fp32, fp32r, int32 = mybir.dt.float32, mybir.dt.float32r, mybir.dt.int32
    ALU = mybir.AluOpType
    ACT = mybir.ActivationFunctionType
    batch = ids.shape[0]
    tiles = batch // P
    assert batch % (2 * P) == 0 and tiles >= 6
    look_rows = tables[LOOKED[0]].shape[0] // PARTS
    assert all(tables[k].shape[0] == look_rows * PARTS for k in LOOKED)
    assert look_rows <= P and look_rows * PARTS <= 4096 and 2 <= LOOKS <= 8 and LOOKS % 2 == 0
    assert FEATURES < 32 and batch <= FEATURES * P

    ctx = ExitStack()
    with ctx:
        def sbuf(name, shape, dt=fp32):
            return ctx.enter_context(nc.sbuf_tensor(name, shape, dt))

        def psum(name, shape):
            return ctx.enter_context(nc.psum_tensor(name, shape, fp32))

        def sem(name):
            return ctx.enter_context(nc.semaphore(name))

        rows = [sbuf(f"rows{u}", [P, len(GATHERED), D]) for u in range(2)]
        index = [sbuf(f"index{u}", [P, TABLES], int32) for u in range(2)]
        turned = sbuf("turned", [D, 2, P, SLOT])
        grams = [sbuf(f"grams{u}", [P, FEATURES, P]) for u in range(2)]
        pairs = [sbuf(f"pairs{u}", [P, CHUNKS, P]) for u in range(2)]
        hidden1 = sbuf("hidden1", [P, L1, P])
        hidden2 = sbuf("hidden2", [P, L2, P])
        y_row = grams[0][32:33].rearrange("p a b -> p (a b)")[:, 0:batch]
        dense_sb = sbuf("dense_sb", [D, batch])
        identity = sbuf("identity", [P, P])
        look_ids = sbuf("look_ids", [P, LOOKS, 2 * P], int32)
        row_number = sbuf("row_number", [P, PARTS], int32)
        table_high = sbuf("table_high", [P, LOOKS, PARTS, D], fp32r)
        table_low = sbuf("table_low", [P, LOOKS, PARTS, D], fp32r)
        looked_sb = sbuf("looked_sb", [D, STAGED, 2 * P])
        match = [sbuf(f"match{b}", [P, PARTS, 2 * P], fp32r) for b in range(2)]
        w1_dense_two = sbuf("w1_dense_two", [D, 2, H1])
        w1_dense_sum = w1_dense_two[:, 0, :]
        w1_pairs_sb = sbuf("w1_pairs_sb", [CHUNK_ROWS, CHUNKS, H1])
        w2_sb = sbuf("w2_sb", [P, L1, H2])
        w3_sb = sbuf("w3_sb", [P, L2])
        b1_sb = sbuf("b1_sb", [P, L1])
        b2_sb = sbuf("b2_sb", [P, L2])
        scratch = [nc.dram_tensor(f"scratch{u}", (FEATURES, FEATURES + SHIFTS, P), fp32).ap() for u in range(2)]

        def raw_table(n):
            place = turned[0:look_rows, 1] if n < 2 else grams[(n - 2) // 3][0:look_rows]
            at = (n if n < 2 else (n - 2) % 3) * PARTS * D
            return place.rearrange("p a b -> p (a b)")[:, at:at + PARTS * D]

        turn_ps = [psum(f"turn_ps{b}", [P, BANK]) for b in range(2)]
        gram_ps = [psum(f"gram_ps{b}", [P, BANK]) for b in range(2)]
        layer1_ps = [psum(f"layer1_ps{h}", [P, L1 // 2, P]) for h in range(2)]
        layer23_ps = psum("layer23_ps", [P, BANK // P, P])
        layer2_ps = layer23_ps[:, 0:L2, :]
        layer3_ps = layer23_ps[0:1, L2, :]
        look_ps = psum("look_ps", [P, BANK])

        index_in = [sem(f"index_in{u}") for u in range(2)]
        look_ids_in = [sem(f"look_ids_in{h}") for h in range(2)]
        raw_table_in = [sem(f"raw_table_in{n}") for n in range(LOOKS)]
        dense_in = sem("dense_in")
        weights_in = sem("weights_in")
        gathered = [[sem(f"gathered{u}_{g}") for g in range(GROUPS)] for u in range(2)]
        tiles_opened = sem("tiles_opened")
        zeroed = sem("zeroed")
        identity_made = sem("identity_made")
        row_numbers_made = sem("row_numbers_made")
        tables_high = sem("tables_high")
        tables_split = sem("tables_split")
        weights_summed = sem("weights_summed")
        turn_done = [sem(f"turn_done{u}") for u in range(2)]
        turned_dve = sem("turned_dve")
        turned_act = sem("turned_act")
        match_ready = sem("match_ready")
        look_done = sem("look_done")
        looked = sem("looked")
        unpacked = sem("unpacked")
        gram_done = sem("gram_done")
        grams_dve = sem("grams_dve")
        grams_act = sem("grams_act")
        scratch_in = [sem(f"scratch_in{u}") for u in range(2)]
        wraps_in = [sem(f"wraps_in{u}") for u in range(2)]
        pairs_in = [sem(f"pairs_in{u}") for u in range(2)]
        layer1_done = sem("layer1_done")
        hidden1_ready = sem("hidden1_ready")
        layer2_done = sem("layer2_done")
        hidden2_ready = sem("hidden2_ready")
        layer3_done = sem("layer3_done")
        y_copied = sem("y_copied")
        y_stored = sem("y_stored")

        READS = CHUNKS * 16

        def after(eng, sem, count):
            if not isinstance(count, int) or count > 0:
                eng.wait_ge(sem, count)

        def bank_of(u, group):
            return (GROUPS * u + group) % 2

        def groups_in_bank(bank, m, u, group):
            return GROUPS * m + (GROUPS * u + group + 1 - bank) // 2

        def next_look(m, r):
            return (m, r + 1) if r + 1 < LOOKS else (m + 1, 0)

        def has_next(m, r):
            return not (isinstance(m, int) and (m, r) == (tiles // 2 - 1, LOOKS - 1))

        block = ctx.enter_context(nc.Block())

        @block.sync
        def _(sp):
            def known(value):
                return value if isinstance(value, int) else sp.snap(sp.to_reg(value))

            def load_index(m, u):
                first = known((2 * m + u) * P)
                after(sp, turn_done[u], known(GROUPS * m))
                sp.dma_start(index[u][:], ids[bass.ds(first, P), :]).then_inc(index_in[u], 16)

            def load_look_ids(m, h):
                row, matched = (known(v) for v in (2 * m + h, LOOKS * (m - 1) + HALF * (h + 1)))
                after(sp, match_ready, matched)
                sp.dma_start(look_ids[:, HALF * h:HALF * (h + 1), :].rearrange("p n s -> p (n s)"),
                             look_ids_rows[bass.ds(row, 1)].broadcast_to([P, HALF * 2 * P])).then_inc(
                                 look_ids_in[h], 16)

            def repack(m, u):
                t = 2 * m + u
                copied, reads, written, layer1s = (
                    known(v) for v in (STEPS * (t + 1), READS * m, 16 * (m + 1), 2 * (t - 1)))
                sp.wait_ge(grams_dve, copied)
                sp.wait_ge(grams_act, copied)
                after(sp, pairs_in[u], reads)
                sp.dma_start(scratch[u][:, 0:FEATURES, :], grams[u][0:FEATURES]).then_inc(scratch_in[u], 16)
                sp.dma_start(scratch[u][WRAPS:, FEATURES:, :],
                             grams[u][WRAPS:FEATURES, 0:SHIFTS, :]).then_inc(wraps_in[u], 16)
                after(sp, layer1_done, layer1s)
                width = FEATURES + SHIFTS
                for c in range(CHUNKS):
                    if c == 0:
                        sp.wait_ge(scratch_in[u], written)
                    if (c + 1) * CHUNK_I > WRAPS >= c * CHUNK_I:
                        sp.wait_ge(wraps_in[u], written)
                    first = c * CHUNK_I * (width + 1) + 1
                    skewed = bass.AP(scratch[u].tensor, first * P, [[(width + 1) * P, CHUNK_I], [P, SHIFTS], [1, P]])
                    sp.dma_start(pairs[u][0:CHUNK_ROWS, c, :], skewed).then_inc(pairs_in[u], 16)

            load_index(0, 0)
            load_look_ids(0, 0)
            load_look_ids(0, 1)
            for n, k in enumerate(LOOKED):
                sp.dma_start(raw_table(n), tables[k].rearrange("(p c) d -> p (c d)", c=PARTS)).then_inc(
                    raw_table_in[n], 16)
            load_index(0, 1)
            sp.wait_ge(raw_table_in[LOOKS - 1], 16)
            sp.dma_start(dense_sb[:], dense_t).then_inc(dense_in, 16)
            sp.dma_start(w1_dense_two[:], w1_dense).then_inc(weights_in, 16)
            sp.dma_start(w1_pairs_sb[:], w1_pairs).then_inc(weights_in, 16)
            sp.dma_start(b1_sb[:], b1).then_inc(weights_in, 16)
            sp.dma_start(w2_sb[:], w2).then_inc(weights_in, 16)
            sp.dma_start(b2_sb[:], b2).then_inc(weights_in, 16)
            sp.dma_start(w3_sb[:], w3).then_inc(weights_in, 16)
            load_look_ids(1, 0)

            def step(m, u, more_ids=True):
                load_index(m, u)
                if more_ids:
                    load_look_ids(m + u, 1 - u)
                repack(m - 1, u)

            last_m = tiles // 2 - 1
            step(1, 0)
            step(1, 1)
            with sp.Fori(2, last_m) as m:
                step(m, 0)
                step(m, 1)
            step(last_m, 0)
            step(last_m, 1, more_ids=False)
            for u in range(2):
                repack(last_m, u)
            sp.wait_ge(y_copied, tiles + 1)
            sp.dma_start(y, y_row).then_inc(y_stored, 16)
            sp.wait_ge(y_stored, 16)

        @block.gpsimd
        def _(pool):
            def gather_tile(m, u):
                after(pool, turn_done[u], GROUPS * m)
                pool.wait_ge(index_in[u], 16 * (m + 1))
                pool.sem_inc(tiles_opened, 1)
                for group in range(GROUPS):
                    for n, k in enumerate(tables_of(group)):
                        pool.indirect_dma_start(
                            out=rows[u][:, group * GROUP_OF + n, :], out_offset=None, in_=tables[k],
                            in_offset=bass.IndirectOffsetOnAxis(ap=index[u][:, k:k + 1], axis=0),
                        ).then_inc(gathered[u][group], 16)

            nc.gpsimd.memset(identity[:], 0.0).then_inc(zeroed, 1)
            pool.wait_ge(zeroed, 1)
            nc.gpsimd.affine_select(out=identity[:], in_=identity[:], compare_op=ALU.not_equal, fill=1.0,
                                    base=0, pattern=[[-1, P]], channel_multiplier=1).then_inc(identity_made, 1)
            nc.gpsimd.iota(row_number[:], pattern=[[1, PARTS]], base=0,
                           channel_multiplier=PARTS).then_inc(row_numbers_made, 1)
            gather_tile(0, 0)
            gather_tile(0, 1)
            with pool.Fori(1, tiles // 2) as m:
                gather_tile(m, 0)
                gather_tile(m, 1)

        @block.tensor
        def _(pe):
            def turn(m, u, group):
                bank = bank_of(u, group)
                after(pe, (turned_dve, turned_act)[bank], groups_in_bank(bank, m, u, group))
                ks = tables_of(group)
                pe.wait_ge(gathered[u][group], 16 * len(ks) * (m + 1))
                for n in range(len(ks)):
                    last = nc.tensor.transpose(turn_ps[bank][:, n * P:(n + 1) * P],
                                               rows[u][:, group * GROUP_OF + n, :], identity[:])
                last.then_inc(turn_done[u], 1)

            def look(m, r):
                if isinstance(m, int) and m == 0:
                    pe.wait_ge(tables_split, r + 1)
                pe.wait_ge(match_ready, LOOKS * m + r + 1)
                after(pe, looked, LOOKS * m + r)
                for c in range(PARTS):
                    for part in (table_high, table_low):
                        last = nc.tensor.matmul(look_ps[:, 0:2 * P], part[0:look_rows, r, c, :],
                                                match[r % 2][0:look_rows, c, :],
                                                start=(c == 0 and part is table_high),
                                                stop=(c == PARTS - 1 and part is table_low))
                last.then_inc(look_done, 1)

            def gram(m, u, step):
                t = 2 * m + u
                if step == 0:
                    pe.wait_ge(turned_dve, groups_in_bank(0, m, u, GROUPS))
                    pe.wait_ge(turned_act, groups_in_bank(1, m, u, GROUPS))
                    pe.wait_ge(unpacked, m + 1)
                    pe.wait_ge(looked, LOOKS * (m + 1))
                after(pe, grams_dve, STEPS * t + step - 1)
                after(pe, grams_act, STEPS * t + step - 1)
                for x in range(IN_QUADRANT):
                    for s in range(4):
                        of_sample = turned[:, u, (step * 4 + s) * IN_QUADRANT + x, 0:FEATURES]
                        last = nc.tensor.matmul(
                            gram_ps[step][s * 32:s * 32 + FEATURES, x * FEATURES:(x + 1) * FEATURES],
                            of_sample, of_sample, start=True, stop=True)
                last.then_inc(gram_done, 1)

            def layer1(m, u):
                pe.wait_ge(pairs_in[u], READS * (m + 1))
                for o in range(L1):
                    nc.tensor.matmul(layer1_ps[o // 2][:, o % 2, :], w1_dense_sum[:, o * P:(o + 1) * P],
                                     dense_sb[:, bass.ts(2 * m + u, P)], start=True, stop=False)
                    for c in range(CHUNKS):
                        last = nc.tensor.matmul(layer1_ps[o // 2][:, o % 2, :], w1_pairs_sb[:, c, o * P:(o + 1) * P],
                                                pairs[u][0:CHUNK_ROWS, c, :],
                                                start=False, stop=(c == CHUNKS - 1))
                    if o % 2 == 1:
                        last.then_inc(layer1_done, 1)

            def layer2(m, u):
                t = 2 * m + u
                pe.wait_ge(hidden1_ready, t + 1)
                pe.wait_ge(y_copied, t + 1)
                for o in range(L2):
                    for c in range(L1):
                        last = nc.tensor.matmul(layer2_ps[:, o, :], w2_sb[:, c, o * P:(o + 1) * P],
                                                hidden1[:, c, :], start=(c == 0), stop=(c == L1 - 1))
                last.then_inc(layer2_done, 1)

            def layer3(m, u):
                pe.wait_ge(hidden2_ready, 2 * m + u + 1)
                for c in range(L2):
                    last = nc.tensor.matmul(layer3_ps, w3_sb[:, c:c + 1], hidden2[:, c, :],
                                            start=(c == 0), stop=(c == L2 - 1))
                last.then_inc(layer3_done, 1)

            def tile(m, u, grams=True, layers=True, looks=True, last=False):
                gm = m - 1 + u
                for group in range(GROUPS):
                    turn(m, u, group)
                    if looks:
                        for look_of in looks_after(m, u, group):
                            look(*look_of)
                    if grams and group < STEPS:
                        gram(gm, 1 - u, group)
                    if layers and group == AT_LAYER[0]:
                        layer1(m - 1, u)
                    if layers and group == AT_LAYER[1] and not last:
                        layer2(m - 1, u)
                    if layers and group == AT_LAYER[2] and not last:
                        layer3(m - 1, u)

            pe.wait_ge(identity_made, 1)
            for r in range(EARLY):
                look(0, r)
            tile(0, 0, grams=False, layers=False)
            tile(0, 1, layers=False)
            pe.wait_ge(weights_summed, 1)
            pe.wait_ge(dense_in, 16)
            last_m = tiles // 2 - 1
            with pe.Fori(1, last_m) as m:
                tile(m, 0)
                tile(m, 1)
            tile(last_m, 0)
            tile(last_m, 1, looks=False, last=True)
            layer2(last_m - 1, 1)
            for step in range(STEPS):
                gram(last_m, 1, step)
            layer1(last_m, 0)
            layer3(last_m - 1, 1)
            layer2(last_m, 0)
            layer1(last_m, 1)
            layer3(last_m, 0)
            layer2(last_m, 1)
            layer3(last_m, 1)

        def take_turned(eng, copy, done, m, u, group):
            eng.wait_ge(turn_done[u], GROUPS * m + group + 1)
            bank = turn_ps[bank_of(u, group)]
            for n, k, length in runs_of(tables_of(group)):
                last = copy(turned[:, u, :, 1 + k:1 + k + length],
                            bank[:, n * P:(n + length) * P].rearrange("d (f s) -> d s f", f=length))
            last.then_inc(done, 1)

        def take_gram(eng, copy, done, quadrants, m, u, step):
            eng.wait_ge(gram_done, STEPS * (2 * m + u) + step + 1)
            if step == 0:
                after(eng, scratch_in[u], 16 * m)
                after(eng, wraps_in[u], 16 * m)
            for s in quadrants:
                sample = (step * 4 + s) * IN_QUADRANT
                last = copy(grams[u][0:FEATURES, :, sample:sample + IN_QUADRANT],
                            gram_ps[step][s * 32:s * 32 + FEATURES, 0:IN_QUADRANT * FEATURES].rearrange(
                                "i (x j) -> i j x", j=FEATURES))
            last.then_inc(done, 1)

        @block.vector
        def _(dve):
            def matches(m, r):
                if r % HALF == 0:
                    dve.wait_ge(look_ids_in[r // HALF], 16 * (m + 1))
                after(dve, look_done, LOOKS * m + r - 1)
                shape = [look_rows, PARTS, 2 * P]
                nc.vector.tensor_tensor(
                    match[r % 2][0:look_rows], look_ids[0:look_rows, r].unsqueeze(1).broadcast_to(shape),
                    row_number[0:look_rows].unsqueeze(2).broadcast_to(shape),
                    ALU.is_equal).then_inc(match_ready, 1)

            def split_low(n):
                dve.wait_ge(tables_high, n + 1)
                nc.vector.tensor_tensor(table_low[0:look_rows, n].rearrange("p c d -> p (c d)"), raw_table(n),
                                        table_high[0:look_rows, n].bitcast(fp32).rearrange("p c d -> p (c d)"),
                                        ALU.subtract).then_inc(tables_split, 1)

            def relu2(m, u):
                dve.wait_ge(layer2_done, 2 * m + u + 1)
                for o in range(L2):
                    last = nc.vector.tensor_scalar(hidden2[:, o, :], layer2_ps[:, o, :], b2_sb[:, o:o + 1], 0.0,
                                                   ALU.add, ALU.max)
                last.then_inc(hidden2_ready, 1)

            def copy_y(m, u):
                t = 2 * m + u
                dve.wait_ge(layer3_done, t + 1)
                nc.vector.tensor_copy(y_row[:, bass.ts(t, P)], layer3_ps).then_inc(y_copied, 1)

            def take_steps(m, u, step):
                take_gram(dve, nc.vector.tensor_copy, grams_dve, (0, 1), m, u, step)

            def tile(m, u, grams=True, layers=True, looks=True, last=False):
                gm = m - 1 + u
                for group in range(GROUPS):
                    if bank_of(u, group) == 0:
                        take_turned(dve, nc.vector.tensor_copy, turned_dve, m, u, group)
                    if looks:
                        for look_of in looks_after(m, u, group):
                            if has_next(*look_of):
                                matches(*next_look(*look_of))
                    if grams and group < STEPS:
                        take_steps(gm, 1 - u, group)
                    if layers and group == AT_LAYER[1] and not last:
                        relu2(m - 1, u)
                    if layers and group == AT_LAYER[2] and not last:
                        copy_y(m - 1, u)

            dve.sem_inc(y_copied, 1)
            dve.wait_ge(row_numbers_made, 1)
            matches(0, 0)
            for n in range(LOOKS):
                split_low(n)
                if n in (2, 5):
                    matches(0, (n + 1) // 3)
            tile(0, 0, grams=False, layers=False)
            dve.wait_ge(weights_in, 6 * 16)
            nc.vector.tensor_tensor(w1_dense_sum, w1_dense_two[:, 0, :], w1_dense_two[:, 1, :],
                                    ALU.add).then_inc(weights_summed, 1)
            tile(0, 1, layers=False)
            last_m = tiles // 2 - 1
            with dve.Fori(1, last_m) as m:
                tile(m, 0)
                tile(m, 1)
            tile(last_m, 0)
            tile(last_m, 1, looks=False, last=True)
            for step in range(STEPS):
                take_steps(last_m, 1, step)
                if step == 0:
                    relu2(last_m - 1, 1)
            copy_y(last_m - 1, 1)
            for u in range(2):
                relu2(last_m, u)
                copy_y(last_m, u)

        @block.scalar
        def _(act):
            def relu1(m, u):
                for o in range(L1):
                    if o % 2 == 0:
                        act.wait_ge(layer1_done, 2 * (2 * m + u) + o // 2 + 1)
                    last = nc.scalar.activation(hidden1[:, o, :], layer1_ps[o // 2][:, o % 2, :], ACT.Relu,
                                                bias=b1_sb[:, o:o + 1])
                last.then_inc(hidden1_ready, 1)

            def split_high(n):
                act.wait_ge(raw_table_in[n], 16)
                nc.scalar.copy(table_high[0:look_rows, n].rearrange("p c d -> p (c d)"),
                               raw_table(n)).then_inc(tables_high, 1)

            def take_look(m, r):
                if r == 0:
                    after(act, unpacked, m)
                act.wait_ge(look_done, LOOKS * m + r + 1)
                if r < STAGED:
                    nc.scalar.copy(looked_sb[:, r, :], look_ps[:, 0:2 * P]).then_inc(looked, 1)
                else:
                    nc.scalar.copy(turned[:, :, :, 1 + LOOKED[r]],
                                   look_ps[:, 0:2 * P].rearrange("d (u s) -> d u s", u=2)).then_inc(looked, 1)

            def unpack(m):
                act.wait_ge(looked, LOOKS * m + STAGED)
                for n in range(STAGED):
                    nc.scalar.copy(turned[:, :, :, 1 + LOOKED[n]],
                                   looked_sb[:, n, :].rearrange("d (u s) -> d u s", u=2))
                nc.scalar.copy(turned[:, :, :, 0],
                               dense_sb[:, bass.ts(m, 2 * P)].rearrange("d (u s) -> d u s", u=2)).then_inc(
                                   unpacked, 1)

            def take_steps(m, u, step):
                take_gram(act, nc.scalar.copy, grams_act, (2, 3), m, u, step)

            def tile(m, u, grams=True, layers=True, looks=True, last=False):
                gm = m - 1 + u
                for group in range(GROUPS):
                    if bank_of(u, group) == 1:
                        take_turned(act, nc.scalar.copy, turned_act, m, u, group)
                    if looks:
                        for look_of in looks_after(m, u, group):
                            take_look(*look_of)
                    if grams and group < STEPS:
                        take_steps(gm, 1 - u, group)
                    if layers and group == AT_LAYER[0]:
                        relu1(m - 1, u)
                    if u == 0 and group == (STEPS - 1 if grams else GROUPS - 3):
                        unpack(m)

            for n in range(LOOKS):
                split_high(n)
            for r in range(EARLY):
                take_look(0, r)
            act.wait_ge(dense_in, 16)
            act.wait_ge(tables_split, 2)
            tile(0, 0, grams=False, layers=False)
            tile(0, 1, layers=False)
            act.wait_ge(weights_in, 6 * 16)
            last_m = tiles // 2 - 1
            with act.Fori(1, last_m) as m:
                tile(m, 0)
                tile(m, 1)
            tile(last_m, 0)
            tile(last_m, 1, looks=False, last=True)
            for step in range(STEPS):
                take_steps(last_m, 1, step)
            for u in range(2):
                relu1(last_m, u)


def kernel(**inputs):
    import concourse.bacc as bacc
    from concourse.bass_utils import run_bass_kernel_spmd

    a = {name: np.ascontiguousarray(value) for name, value in inputs.items()}
    w1, w2, w3 = a["W_top1"], a["W_top2"], a["W_top3"]
    batch = a["ids"].shape[0]

    n_pairs = FEATURES * (FEATURES - 1) // 2
    w1_dense = np.stack([w1[:D], w1[D + n_pairs:]], axis=1)
    row_of = {}
    for i in range(FEATURES):
        for j in range(i + 1, FEATURES):
            row_of[i, j] = D + len(row_of)
    order = [row_of[min(i, (i + s) % FEATURES), max(i, (i + s) % FEATURES)]
             for i in range(FEATURES) for s in range(1, SHIFTS + 1)]
    w1_pairs = w1[order].reshape(CHUNKS, CHUNK_ROWS, H1).transpose(1, 0, 2)

    look_ids_rows = a["ids"][:, LOOKED].reshape(batch // (2 * P), 2 * P, 2, HALF).transpose(0, 2, 3, 1)
    look_ids_rows = look_ids_rows.reshape(-1, HALF * 2 * P)

    arrays = {
        "dense_t": a["r_dense_features"].T, "ids": a["ids"], "look_ids_rows": look_ids_rows,
        **{f"table{k}": a[f"tbl_{k}"] for k in range(TABLES)},
        "w1_dense": w1_dense, "w1_pairs": w1_pairs, "b1": a["b_top1"].reshape(L1, P).T,
        "w2": w2.reshape(L1, P, H2).transpose(1, 0, 2), "b2": a["b_top2"].reshape(L2, P).T,
        "w3": w3.reshape(L2, P).T,
    }
    arrays = {name: np.ascontiguousarray(v) for name, v in arrays.items()}
    nc = bacc.Bacc("TRN2", target_bir_lowering=False, num_devices=1)
    ap = {name: nc.dram_tensor(f"in_{name}", v.shape, mybir.dt.from_np(v.dtype), kind="ExternalInput").ap()
          for name, v in arrays.items()}
    y = nc.dram_tensor("out_y", (1, batch), mybir.dt.float32, kind="ExternalOutput").ap()
    build(nc, ap["dense_t"], ap["ids"], ap["look_ids_rows"], [ap[f"table{k}"] for k in range(TABLES)],
          ap["w1_dense"], ap["w1_pairs"], ap["b1"], ap["w2"], ap["b2"], ap["w3"], y)
    result = run_bass_kernel_spmd(nc, [{f"in_{name}": v for name, v in arrays.items()}], core_ids=[0])
    return result.results[0]["out_y"].reshape(batch, 1)
```
